# Optimizing a Trainium2 kernel written in Bass

```python
import numpy as np
import jax
import jax.numpy as jnp

def _softmax(x, axis=-1):
    return jax.nn.softmax(x, axis=axis)

def _gelu(x):
    return jax.nn.gelu(x, approximate=True)

def _silu(x):
    return jax.nn.silu(x)

def _sigmoid(x):
    return jax.nn.sigmoid(x)

def _layernorm(x, axis=-1, eps=1e-05):
    m = jnp.mean(x, axis=axis, keepdims=True)
    v = jnp.var(x, axis=axis, keepdims=True)
    return (x - m) / jnp.sqrt(v + eps)

def _scatter_add(tgt, idx, src, axis=0):
    return tgt.at[idx].add(src)

def _segment_sum(src, seg, n):
    return jax.ops.segment_sum(src, seg, n)
kernel_name = 'mk_adaln_ffn_d1_seqx_r8_3508ba'

def setup_inputs(seed: int=0):
    np.random.seed(seed)
    _w = jnp.asarray

    def _rec_inputs():
        import jax
        import jax.numpy as jnp
        _rk = jax.random.key(seed)
        x = -7.109e-05 + 0.9999 * jax.random.normal(jax.random.fold_in(_rk, 1), (32, 32, 256), jnp.float32)
        _lenS = 32 - jax.random.randint(jax.random.fold_in(_rk, 7), (32,), 0, max(1, 32 // 4) + 1, jnp.int32)
        _lenS2 = 32 - jax.random.randint(jax.random.fold_in(_rk, 8), (32,), 0, max(1, 32 // 4) + 1, jnp.int32)
        itok_B_1_198 = jax.random.randint(jax.random.fold_in(_rk, 11), (32,), 1, 199, jnp.int32)
        return (x, itok_B_1_198)
    x, itok_B_1_198 = _rec_inputs()

    def _L0_cond_setup():
        import jax, jax.numpy as jnp
        import numpy as np
        B, C, T = (128, 32, 256)
        S, D = (200, 32)
        key = jax.random.key(seed)
        k1, k2, k3 = jax.random.split(key, 3)
        x = jax.random.normal(k1, (B, C, T), dtype=jnp.float32)
        conditions = jax.random.randint(k2, (B,), 0, S, dtype=jnp.int64)
        weights = jax.random.normal(k3, (S, C, D), dtype=jnp.float32) / jnp.sqrt(jnp.float32(C))
        return {'x': x, 'conditions': conditions, 'weights': weights}
    _L0_cond_all = _L0_cond_setup()
    _L0_cond_in = {k: v for k, v in _L0_cond_all.items() if k in ('weights',)}
    del _L0_cond_all

    def _L0_ffn_setup():
        import jax, jax.numpy as jnp
        import numpy as np
        TOP_K = 4
        key = jax.random.key(seed)
        ks = jax.random.split(key, 8)
        B, S, D, E, H, HS = (2, 256, 256, 16, 128, 512)
        scaled = lambda k, shape, fan: jax.random.normal(k, shape, jnp.float32) * fan ** (-0.5)
        return {'x': jax.random.normal(ks[0], (B, S, D), jnp.float32), 'w_router': scaled(ks[1], (D, E), D), 'we1': scaled(ks[2], (E, D, H), D), 'we3': scaled(ks[3], (E, D, H), D), 'we2': scaled(ks[4], (E, H, D), H), 'ws1': scaled(ks[5], (D, HS), D), 'ws3': scaled(ks[6], (D, HS), D), 'ws2': scaled(ks[7], (HS, D), HS)}
    _L0_ffn_all = _L0_ffn_setup()
    _L0_ffn_in = {k: v for k, v in _L0_ffn_all.items() if k in ('w_router', 'we1', 'we3', 'we2', 'ws1', 'ws3', 'ws2')}
    del _L0_ffn_all
    return {'x': x, 'itok_B_1_198': itok_B_1_198, 'L0_cond_weights': _L0_cond_in['weights'], 'L0_ffn_w_router': _L0_ffn_in['w_router'], 'L0_ffn_we1': _L0_ffn_in['we1'], 'L0_ffn_we3': _L0_ffn_in['we3'], 'L0_ffn_we2': _L0_ffn_in['we2'], 'L0_ffn_ws1': _L0_ffn_in['ws1'], 'L0_ffn_ws3': _L0_ffn_in['ws3'], 'L0_ffn_ws2': _L0_ffn_in['ws2']}

def reference(x, itok_B_1_198, L0_cond_weights, L0_ffn_w_router, L0_ffn_we1, L0_ffn_we3, L0_ffn_we2, L0_ffn_ws1, L0_ffn_ws3, L0_ffn_ws2):
    import jax
    import jax.numpy as jnp

    def _L0_cond_ref(x, conditions, weights):
        import jax, jax.numpy as jnp
        import numpy as np
        B, C, T = (128, 32, 256)
        S, D = (200, 32)
        w = weights[conditions]
        return jnp.einsum('bct,bcd->bdt', x, w)

    def _L0_ffn_ref(x, w_router, we1, we3, we2, ws1, ws3, ws2):
        import jax, jax.numpy as jnp
        import numpy as np
        TOP_K = 4
        B, S, D = x.shape
        T = B * S
        E = w_router.shape[1]
        xt = x.reshape(T, D)
        probs = jax.nn.softmax(xt @ w_router, axis=-1)
        top_w, top_i = jax.lax.top_k(probs, TOP_K)
        top_w = top_w / jnp.sum(top_w, axis=-1, keepdims=True)
        cw = jnp.zeros((T, E), xt.dtype).at[jnp.arange(T)[:, None], top_i].add(top_w)
        g = jax.nn.silu(jnp.einsum('td,edh->teh', xt, we1)) * jnp.einsum('td,edh->teh', xt, we3)
        g = g * cw[:, :, None]
        moe_out = jnp.einsum('teh,ehd->td', g, we2)
        shared = jax.nn.silu(xt @ ws1) * (xt @ ws3) @ ws2
        k = TOP_K
        out = shared / (k + 1) + moe_out * (k / (k + 1))
        return out.reshape(B, S, D)
    x = x + _L0_ffn_ref(_L0_cond_ref(x, itok_B_1_198, L0_cond_weights), L0_ffn_w_router, L0_ffn_we1, L0_ffn_we3, L0_ffn_we2, L0_ffn_ws1, L0_ffn_ws3, L0_ffn_ws2)
    return x

_drawn_inputs = setup_inputs


def setup_inputs(seed=0):
    import zlib

    import numpy as np

    out = dict(_drawn_inputs(seed))
    spreads = {}
    factors = {}
    for name, (base, spread) in spreads.items():
        noise = np.random.default_rng([zlib.crc32(name.encode()), seed]).standard_normal(out[name].shape)
        drawn = base * np.exp(spread * noise) if base else spread * noise
        out[name] = jnp.asarray(drawn.astype(out[name].dtype))
    for name, factor in factors.items():
        out[name] = (out[name] * factor).astype(out[name].dtype)
    return out
```

```python
from contextlib import ExitStack

import numpy as np

import concourse.bass as bass
from concourse import mybir

ALU = mybir.AluOpType
ACT = mybir.ActivationFunctionType
AX = mybir.AxisListType
F32 = mybir.dt.float32
F32R = mybir.dt.float32r
I32 = mybir.dt.int32
U32 = mybir.dt.uint32

P = 128
TOP_K = 4


def adaln_ffn(nc, x, itok, cond_w, w_router, we1, we3, we2, ws1, ws3, ws2, out):
    B, C, D = x.shape
    S = cond_w.shape[0]
    E, _, H = we1.shape
    HS = ws1.shape[1]
    T = B * C
    KD = D // P
    TT = T // P
    Q = P // C
    HALF = T // 2
    TH = HALF // P
    NSH = HS // H
    UNITS = NSH + E
    WC = 2 * KD * H + D
    SLOTS = 4
    assert NSH == SLOTS and E % SLOTS == 0 and H == P and HALF == 512 and TH == 4

    with ExitStack() as ctx:
        def sb(name, shape, dt=F32):
            return ctx.enter_context(nc.sbuf_tensor(name, shape, dt))

        def sem(name):
            return ctx.enter_context(nc.semaphore(name))

        acc = sb("acc", [P, TT, D])
        itok_all = sb("itok_all", [P, B], I32)
        chan = sb("chan", [P, Q])
        chan_i = sb("chan_i", [P, Q], I32)
        gather_idx = sb("gather_idx", [P, TT], I32)
        cond_g = sb("cond_g", [P, TT, C])
        cond_bd = sb("cond_bd", [P, TT, P])
        y_hi = sb("y_hi", [P, KD, T], F32R)
        y_lo = sb("y_lo", [P, KD, T], F32R)
        wr = sb("wr", [P, KD, E])
        wr_hi = sb("wr_hi", [P, KD, E], F32R)
        wr_lo = sb("wr_lo", [P, KD, E], F32R)
        w_raw = sb("w_raw", [P, SLOTS, WC])
        zeros = sb("zeros", [P, WC])
        w_hi = sb("w_hi", [P, SLOTS, WC], F32R)
        w_lo = sb("w_lo", [P, SLOTS, WC], F32R)
        sil = sb("sil", [P, 2, HALF])
        g = sb("g", [P, 2, HALF])
        g_hi = sb("g_hi", [P, 2, HALF], F32R)
        g_lo = sb("g_lo", [P, 2, HALF], F32R)
        lg = sb("lg", [P, TT, E])
        lmax = sb("lmax", [P, TT])
        prob = sb("prob", [P, TT, E])
        psumv = sb("psumv", [P, TT])
        prec = sb("prec", [P, TT])
        top_v = sb("top_v", [P, TT, 8])
        top_i = sb("top_i", [P, TT, 8], U32)
        top_f = sb("top_f", [P, TT, 8])
        top_s = sb("top_s", [P, TT])
        top_r = sb("top_r", [P, TT])
        iota_i = sb("iota_i", [P, E], I32)
        iota_e = sb("iota_e", [P, E])
        pick = sb("pick", [P, TT, E])
        mask = sb("mask", [P, TT, E])
        cw = sb("cw", [P, E, TT])

        gate_ps = [ctx.enter_context(nc.psum_tensor(f"gate_ps{h}", [P, HALF], F32)) for h in range(2)]
        up_ps = [ctx.enter_context(nc.psum_tensor(f"up_ps{h}", [P, HALF], F32)) for h in range(2)]
        down_ps = [[ctx.enter_context(nc.psum_tensor(f"down_ps{h}{j}", [P, 2, D], F32)) for j in range(2)]
                   for h in range(2)]
        y_ps = [[gate_ps[h], up_ps[h]] for h in range(2)]
        lg_ps = down_ps[1][1]

        x_in = [sem(f"x_in{h}") for h in range(2)]
        itok_in = sem("itok_in")
        wr_in = sem("wr_in")
        iota_done = sem("iota_done")
        idx_done = sem("idx_done")
        gathered = [sem(f"gathered{h}") for h in range(2)]
        bd_zero = sem("bd_zero")
        bd_done = sem("bd_done")
        cond_done = sem("cond_done")
        y_hi_done = sem("y_hi_done")
        y_lo_done = sem("y_lo_done")
        wr_hi_done = sem("wr_hi_done")
        wr_lo_done = sem("wr_lo_done")
        lg_done = sem("lg_done")
        route = sem("route")
        exp_in = sem("exp_in")
        exp_done = sem("exp_done")
        w_in = [sem(f"w_in{k}") for k in range(SLOTS)]
        w_hi_done = sem("w_hi_done")
        w_split = sem("w_split")
        gate_done = sem("gate_done")
        up_done = sem("up_done")
        silu_done = sem("silu_done")
        g_done = sem("g_done")
        g_hi_done = sem("g_hi_done")
        g_lo_done = sem("g_lo_done")
        down_done = sem("down_done")
        added = sem("added")
        out_done = sem("out_done")

        x_tiles = x.rearrange("(g q) c t -> (q c) g t", q=Q)
        out_tiles = out.rearrange("(g q) c t -> (q c) g t", q=Q)
        cond_rows = cond_w.rearrange("s c d -> (s c) d")

        def w13(w, slot, m, k):
            at = (m * KD + k) * H
            return w[:, slot, at:at + H]

        def w2(w, slot):
            return w[:, slot, 2 * KD * H:WC]

        def groups(body):
            def run(eng):
                body(eng, 0, None)
                with eng.Fori(0, E // SLOTS) as i:
                    body(eng, (i + 1) * SLOTS, i * SLOTS)
            return run

        block = ctx.enter_context(nc.Block())

        @block.sync
        def _(sp):
            for h in range(2):
                sp.dma_start(acc[:, TH * h:TH * h + TH, :], x_tiles[:, TH * h:TH * h + TH, :]).then_inc(x_in[h], 16)

            def load(eng, unit, expert):
                for k in range(SLOTS):
                    n = unit + k
                    if expert is None:
                        s1, s3 = (w.rearrange("(k p) (s h) -> s p k h", p=P, h=H)[k] for w in (ws1, ws3))
                        s2 = ws2[k * H:(k + 1) * H, :]
                    else:
                        eng.wait_ge(w_split, n - SLOTS + 1)
                        s1, s3 = (w.rearrange("e (k p) h -> e p k h", p=P)[bass.ds(expert + k, 1)]
                                  .rearrange("e p k h -> (e p) k h") for w in (we1, we3))
                        s2 = we2[bass.ds(expert + k, 1)].rearrange("e h d -> (e h) d")
                    for m, s in enumerate((s1, s3)):
                        dst = w_raw[:, k, m * KD * H:(m + 1) * KD * H].rearrange("p (k h) -> p k h", k=KD)
                        eng.dma_start(dst, s).then_inc(w_in[k], 16)
                    eng.dma_start(w2(w_raw, k), s2).then_inc(w_in[k], 16)

            groups(load)(sp)
            for h in range(2):
                for j in range(2):
                    sp.wait_ge(added, 4 * (UNITS - 1) + 2 * h + j + 1)
                    t = TH * h + 2 * j
                    sp.dma_start(out_tiles[:, t:t + 2, :], acc[:, t:t + 2, :]).then_inc(out_done, 16)
            sp.wait_ge(out_done, 16 * 4)

        @block.gpsimd
        def _(pool):
            pool.iota(chan_i[:, :], pattern=[[-C, Q]], base=0, channel_multiplier=1).then_inc(iota_done, 1)
            pool.wait_ge(iota_done, 1)
            pool.iota(iota_i[:, :], pattern=[[1, E]], base=0, channel_multiplier=0).then_inc(iota_done, 1)
            pool.wait_ge(idx_done, Q)
            for t in range(TT):
                pool.indirect_dma_start(
                    cond_g[:, t, :], None, cond_rows,
                    bass.IndirectOffsetOnAxis(ap=gather_idx[:, t:t + 1], axis=0),
                ).then_inc(gathered[t // TH], 16)

            def split(eng, unit, expert):
                for k in range(SLOTS):
                    n = unit + k
                    eng.wait_ge(w_in[k], 48 * ((unit + SLOTS) // SLOTS) if expert is None else (expert + 2 * SLOTS) * (48 // SLOTS))
                    if expert is not None:
                        eng.wait_ge(down_done, 4 * (n - SLOTS + 1))
                    eng.tensor_tensor(w_hi[:, k, :], w_raw[:, k, :], zeros[:, :], ALU.add).then_inc(w_hi_done, 1)
                    eng.wait_ge(w_hi_done, n + 1)
                    eng.tensor_tensor(w_lo[:, k, :], w_raw[:, k, :], w_hi[:, k, :].bitcast(F32), ALU.subtract).then_inc(w_split, 1)

            pool.wait_ge(bd_zero, 2)
            groups(split)(pool)

        @block.scalar
        def _(act):
            act.dma_start(itok_all[:, :], itok.rearrange("(a b) -> a b", a=1).to_broadcast((P, B))).then_inc(itok_in, 16)
            act.dma_start(wr[:, :, :], w_router.rearrange("(k p) e -> p k e", p=P)).then_inc(wr_in, 16)
            act.wait_ge(wr_in, 16)
            act.activation(wr_hi[:, :, :], wr[:, :, :], ACT.Copy).then_inc(wr_hi_done, 1)
            for h in range(2):
                act.wait_ge(cond_done, h + 1)
                for k in range(KD):
                    act.activation(y_hi[:, k, h * HALF:(h + 1) * HALF], y_ps[h][k][:, :], ACT.Copy).then_inc(y_hi_done, 1)
            act.wait_ge(exp_in, 1)
            act.activation(prob[:, :, :], lg[:, :, :], ACT.Exp).then_inc(exp_done, 1)

            def activations(eng, unit, expert):
                for k in range(SLOTS):
                    for h in range(2):
                        s = (unit + k) * 2 + h
                        first = expert is None and k == 0
                        eng.wait_ge(gate_done, s + 1)
                        if not first:
                            eng.wait_ge(g_done, s - 1)
                        eng.activation(sil[:, h, :], gate_ps[h][:, :], ACT.Silu).then_inc(silu_done, 1)
                        eng.wait_ge(g_done, s + 1)
                        if not first:
                            eng.wait_ge(down_done, 2 * (s - 1))
                        eng.activation(g_hi[:, h, :], g[:, h, :], ACT.Copy).then_inc(g_hi_done, 1)

            groups(activations)(act)

        @block.vector
        def _(dve):
            dve.memset(cond_bd[:, :, :], 0.0).then_inc(bd_zero, 1)
            dve.memset(zeros[:, :], 0.0).then_inc(bd_zero, 1)
            dve.wait_ge(iota_done, 2)
            dve.tensor_copy(chan[:, :], chan_i[:, :]).then_inc(route, 1)
            dve.tensor_copy(iota_e[:, :], iota_i[:, :]).then_inc(route, 1)
            dve.wait_ge(route, 2)
            dve.wait_ge(itok_in, 16)
            for q in range(Q):
                r = slice(q * C, (q + 1) * C)
                dve.tensor_scalar(gather_idx[r, :], itok_all[r, q::Q], float(C), chan[r, q:q + 1], ALU.mult, ALU.add).then_inc(idx_done, 1)
            dve.wait_ge(wr_hi_done, 1)
            dve.tensor_tensor(wr_lo[:, :, :], wr[:, :, :], wr_hi[:, :, :].bitcast(F32), ALU.subtract).then_inc(wr_lo_done, 1)
            dve.wait_ge(bd_zero, 1)
            for h in range(2):
                dve.wait_ge(gathered[h], 16 * TH)
                for q in range(Q):
                    r = slice(q * C, (q + 1) * C)
                    t = slice(TH * h, TH * h + TH)
                    dve.tensor_copy(cond_bd[r, t, r], cond_g[r, t, :]).then_inc(bd_done, 1)
            for h in range(2):
                for k in range(KD):
                    dve.wait_ge(y_hi_done, KD * h + k + 1)
                    r = slice(h * HALF, (h + 1) * HALF)
                    dve.tensor_tensor(y_lo[:, k, r], y_ps[h][k][:, :], y_hi[:, k, r].bitcast(F32), ALU.subtract).then_inc(y_lo_done, 1)

            done = [2]

            def chain(ins):
                done[0] += 1
                ins.then_inc(route, 1)
                dve.wait_ge(route, done[0])

            def over_e(v):
                return v.rearrange("p (t a) -> p t a", a=1).to_broadcast((P, TT, E))

            dve.wait_ge(lg_done, 1)
            lg_v = lg_ps[:, 0, 0:TT * E].rearrange("p (t e) -> p t e", e=E)
            chain(dve.tensor_reduce(lmax[:, :], lg_v, AX.X, ALU.max))
            dve.tensor_tensor(lg[:, :, :], lg_v, over_e(lmax[:, :]), ALU.subtract).then_inc(exp_in, 1)
            dve.wait_ge(exp_done, 1)
            chain(dve.tensor_reduce(psumv[:, :], prob[:, :, :], AX.X, ALU.add))
            chain(dve.reciprocal(prec[:, :], psumv[:, :]))
            chain(dve.tensor_tensor(prob[:, :, :], prob[:, :, :], over_e(prec[:, :]), ALU.mult))
            for t in range(TT):
                chain(dve.max(top_v[:, t, :], prob[:, t, :]))
                chain(dve.max_index(top_i[:, t, :], top_v[:, t, :], prob[:, t, :]))
            chain(dve.tensor_copy(top_f[:, :, :], top_i[:, :, :]))
            chain(dve.tensor_reduce(top_s[:, :], top_v[:, :, 0:TOP_K], AX.X, ALU.add))
            chain(dve.reciprocal(top_r[:, :], top_s[:, :]))
            chain(dve.tensor_scalar(top_r[:, :], top_r[:, :], TOP_K / (TOP_K + 1.0), None, ALU.mult))
            iota_v = iota_e[:, :].rearrange("p (a e) -> p a e", a=1).to_broadcast((P, TT, E))
            for k in range(TOP_K):
                to = mask if k == 0 else pick
                chain(dve.tensor_tensor(to[:, :, :], iota_v, over_e(top_f[:, :, k]), ALU.is_equal))
                if k:
                    chain(dve.tensor_tensor(mask[:, :, :], mask[:, :, :], pick[:, :, :], ALU.add))
            chain(dve.tensor_tensor(mask[:, :, :], mask[:, :, :], prob[:, :, :], ALU.mult))
            chain(dve.tensor_tensor(cw[:, :, :].rearrange("p e t -> p t e"), mask[:, :, :], over_e(top_r[:, :]), ALU.mult))

            def add(eng, unit, expert, k, h):
                s = (unit + k) * 2 + h
                for j in range(2):
                    eng.wait_ge(down_done, 2 * s + j + 1)
                    for i in range(2):
                        t = TH * h + 2 * j + i
                        scale = 1.0 / (TOP_K + 1) if expert is None else \
                            cw[:, bass.ds(expert + k, 1), t:t + 1].rearrange("p a b -> p (a b)")
                        ins = eng.scalar_tensor_tensor(out=acc[:, t, :], in0=down_ps[h][j][:, i, :], scalar=scale,
                                                       in1=acc[:, t, :], op0=ALU.mult, op1=ALU.add)
                    ins.then_inc(added, 1)

            def gates(eng, unit, expert):
                for k in range(SLOTS):
                    for h in range(2):
                        s = (unit + k) * 2 + h
                        first = expert is None and k == 0
                        eng.wait_ge(silu_done, s + 1)
                        eng.wait_ge(up_done, s + 1)
                        if not first:
                            eng.wait_ge(g_hi_done, s - 1)
                            eng.wait_ge(g_lo_done, s - 1)
                        eng.tensor_tensor(g[:, h, :], sil[:, h, :], up_ps[h][:, :], ALU.mult).then_inc(g_done, 1)
                        eng.wait_ge(g_hi_done, s + 1)
                        if not first:
                            eng.wait_ge(down_done, 2 * (s - 1))
                        eng.tensor_tensor(g_lo[:, h, :], g[:, h, :], g_hi[:, h, :].bitcast(F32), ALU.subtract).then_inc(g_lo_done, 1)
                        add(eng, unit, expert, k, h)

            groups(gates)(dve)

        @block.tensor
        def _(pe):
            for h in range(2):
                pe.wait_ge(x_in[h], 16)
                pe.wait_ge(bd_done, Q * (h + 1))
                for t in range(TH * h, TH * h + TH):
                    for k in range(KD):
                        c = (t % TH) * P
                        last = pe.matmul(y_ps[h][k][:, c:c + P], acc[:, t, k * P:(k + 1) * P], cond_bd[:, t, :],
                                         start=True, stop=True)
                last.then_inc(cond_done, 1)
            pe.wait_ge(wr_hi_done, 1)
            pe.wait_ge(wr_lo_done, 1)
            pe.wait_ge(y_hi_done, 2 * KD)
            pe.wait_ge(y_lo_done, 2 * KD)
            for t in range(TT):
                for n, (a, b) in enumerate([(y_hi, wr_hi), (y_lo, wr_hi), (y_hi, wr_lo)]):
                    for k in range(KD):
                        last = pe.matmul(lg_ps[:, 0, t * E:(t + 1) * E], a[:, k, t * P:(t + 1) * P], b[:, k, :],
                                         start=(n == 0 and k == 0), stop=(n == 2 and k == KD - 1))
            last.then_inc(lg_done, 1)

            pairs = [(w_hi, y_hi), (w_hi, y_lo), (w_lo, y_hi)]

            def down(eng, unit, k, h, first):
                s = (unit + k) * 2 + h
                eng.wait_ge(g_hi_done, s + 1)
                eng.wait_ge(g_lo_done, s + 1)
                for j in range(2):
                    if not first:
                        eng.wait_ge(added, 2 * (s - 2) + j + 1)
                    for i in range(2):
                        c = (2 * j + i) * P
                        for n, (a, b) in enumerate([(g_hi, w_hi), (g_hi, w_lo), (g_lo, w_hi)]):
                            last = eng.matmul(down_ps[h][j][:, i, :], a[:, h, c:c + P], w2(b, k), start=(n == 0), stop=(n == 2))
                    last.then_inc(down_done, 1)

            def products(eng, unit, expert):
                for k in range(SLOTS):
                    eng.wait_ge(w_split, unit + k + 1)
                    for h in range(2):
                        s = (unit + k) * 2 + h
                        first = expert is None and k == 0
                        for m, (ps, free, ready) in enumerate([(gate_ps, silu_done, gate_done), (up_ps, g_done, up_done)]):
                            if not first:
                                eng.wait_ge(free, s - 1)
                            n = 0
                            for kd in range(KD):
                                for a, b in pairs:
                                    last = eng.matmul(ps[h][:, :], w13(a, k, m, kd), b[:, kd, h * HALF:(h + 1) * HALF],
                                                      start=(n == 0), stop=(n == 3 * KD - 1))
                                    n += 1
                            last.then_inc(ready, 1)
                        down(eng, unit, k, h, first)

            groups(products)(pe)

    return nc


_INS = ["x", "itok_B_1_198", "L0_cond_weights", "L0_ffn_w_router", "L0_ffn_we1", "L0_ffn_we3", "L0_ffn_we2",
        "L0_ffn_ws1", "L0_ffn_ws3", "L0_ffn_ws2"]


def kernel(**inputs):
    import concourse.bacc as bacc
    from concourse.bass_utils import run_bass_kernel_spmd

    nc = bacc.Bacc("TRN2", target_bir_lowering=False, num_devices=1)
    arrays, args = {}, []
    for name in _INS:
        a = np.ascontiguousarray(inputs[name])
        arrays[f"in_{name}"] = a
        args.append(nc.dram_tensor(f"in_{name}", a.shape, mybir.dt.from_np(a.dtype), kind="ExternalInput").ap())
    out = nc.dram_tensor("out", inputs["x"].shape, F32, kind="ExternalOutput").ap()
    adaln_ffn(nc, *args, out)
    return run_bass_kernel_spmd(nc, [arrays], core_ids=[0]).results[0]["out"]
```

```python
from contextlib import ExitStack

import numpy as np

import concourse.bass as bass
from concourse import mybir

ALU = mybir.AluOpType
ACT = mybir.ActivationFunctionType
AX = mybir.AxisListType
F32 = mybir.dt.float32
F32R = mybir.dt.float32r
I32 = mybir.dt.int32
U32 = mybir.dt.uint32

P = 128
TOP_K = 4


def adaln_ffn(nc, x, itok, cond_w, w_router, we1, we3, we2, ws1, ws3, ws2, out):
    B, C, D = x.shape
    S = cond_w.shape[0]
    E, _, H = we1.shape
    HS = ws1.shape[1]
    T = B * C
    KD = D // P
    TT = T // P
    Q = P // C
    HALF = T // 2
    TH = HALF // P
    NSH = HS // H
    UNITS = NSH + E
    WC = 2 * KD * H + D
    SLOTS = 4
    EXP_STEP = 2
    LEAD = 2
    assert NSH == SLOTS and E % SLOTS == 0 and H == P and HALF == 512 and TH == 4

    with ExitStack() as ctx:
        def sb(name, shape, dt=F32):
            return ctx.enter_context(nc.sbuf_tensor(name, shape, dt))

        def sem(name):
            return ctx.enter_context(nc.semaphore(name))

        acc = sb("acc", [P, TT, D])
        itok_all = sb("itok_all", [P, B], I32)
        chan = sb("chan", [P, Q])
        chan_i = sb("chan_i", [P, Q], I32)
        gather_idx = sb("gather_idx", [P, TT], I32)
        cond_g = sb("cond_g", [P, TT, C])
        cond_bd = sb("cond_bd", [P, TT, P])
        y_hi = sb("y_hi", [P, KD, T], F32R)
        y_lo = sb("y_lo", [P, KD, T], F32R)
        wr = sb("wr", [P, KD, E])
        wr_pair = sb("wr_pair", [P, KD, 2, E], F32R)
        lgt = sb("lgt", [2 * E, T])
        ident = sb("ident", [2 * E, 2 * E])
        w_raw = sb("w_raw", [P, SLOTS, WC])
        zeros = sb("zeros", [P, WC])
        w_hi = sb("w_hi", [P, SLOTS, WC], F32R)
        w_lo = sb("w_lo", [P, SLOTS, WC], F32R)
        sil = sb("sil", [P, 2, HALF])
        g = sb("g", [P, 2, HALF])
        g_hi = sb("g_hi", [P, 2, HALF], F32R)
        g_lo = sb("g_lo", [P, 2, HALF], F32R)
        lg = sb("lg", [P, TT, E])
        lmax = sb("lmax", [P, TT])
        prob = sb("prob", [P, TT, E])
        psumv = sb("psumv", [P, TT])
        prec = sb("prec", [P, TT])
        top_v = sb("top_v", [P, TT, 8])
        top_i = sb("top_i", [P, TT, 8], U32)
        top_f = sb("top_f", [P, TT, TOP_K])
        top_s = sb("top_s", [P, TT])
        top_r = sb("top_r", [P, TT])
        iota_i = sb("iota_i", [P, E], I32)
        iota_e = sb("iota_e", [P, E])
        pick = sb("pick", [P, TT, TOP_K, E])
        mask = sb("mask", [P, TT, E])
        cw = sb("cw", [P, UNITS, TT])

        gate_ps = [ctx.enter_context(nc.psum_tensor(f"gate_ps{h}", [P, HALF], F32)) for h in range(2)]
        up_ps = [ctx.enter_context(nc.psum_tensor(f"up_ps{h}", [P, HALF], F32)) for h in range(2)]
        down_ps = [[ctx.enter_context(nc.psum_tensor(f"down_ps{h}{j}", [P, 2, D], F32)) for j in range(2)]
                   for h in range(2)]
        y_ps = [[gate_ps[h], up_ps[h]] for h in range(2)]
        lgt_ps = [down_ps[1][j][0:2 * E, :, :].rearrange("p i d -> p (i d)") for j in range(2)]
        lg_ps = down_ps[1][1]

        x_in = [sem(f"x_in{h}") for h in range(2)]
        itok_in = sem("itok_in")
        wr_in = sem("wr_in")
        iota_done = sem("iota_done")
        idx_done = sem("idx_done")
        gathered = [sem(f"gathered{h}") for h in range(2)]
        bd_zero = sem("bd_zero")
        bd_done = sem("bd_done")
        cond_done = sem("cond_done")
        y_hi_done = sem("y_hi_done")
        y_lo_done = sem("y_lo_done")
        wr_hi_done = sem("wr_hi_done")
        wr_lo_done = sem("wr_lo_done")
        ident_done = sem("ident_done")
        lgt_done = sem("lgt_done")
        lgt_out = sem("lgt_out")
        lg_done = sem("lg_done")
        route = sem("route")
        exp_in = sem("exp_in")
        exp_done = sem("exp_done")
        w_in = [sem(f"w_in{k}") for k in range(SLOTS)]
        lead_hi = sem("lead_hi")
        lead_split = sem("lead_split")
        w_hi_done = sem("w_hi_done")
        w_split = sem("w_split")
        gate_done = sem("gate_done")
        up_done = sem("up_done")
        silu_done = sem("silu_done")
        g_done = sem("g_done")
        g_hi_done = sem("g_hi_done")
        g_lo_done = sem("g_lo_done")
        down_done = sem("down_done")
        added = sem("added")
        out_done = sem("out_done")

        x_tiles = x.rearrange("(g q) c t -> (q c) g t", q=Q)
        out_tiles = out.rearrange("(g q) c t -> (q c) g t", q=Q)
        cond_rows = cond_w.rearrange("s c d -> (s c) d")

        def w13(w, slot, m, k):
            at = (m * KD + k) * H
            return w[:, slot, at:at + H]

        def w2(w, slot):
            return w[:, slot, 2 * KD * H:WC]

        def groups(body):
            def run(eng):
                body(eng, 0, None)
                with eng.Fori(0, E // SLOTS) as i:
                    body(eng, (i + 1) * SLOTS, i * SLOTS)
            return run

        block = ctx.enter_context(nc.Block())

        @block.sync
        def _(sp):
            sp.dma_start(itok_all[:, :], itok.rearrange("(a b) -> a b", a=1).to_broadcast((P, B))).then_inc(itok_in, 16)
            for h in range(2):
                sp.dma_start(acc[:, TH * h:TH * h + TH, :], x_tiles[:, TH * h:TH * h + TH, :]).then_inc(x_in[h], 16)

            def load(eng, unit, expert):
                for k in range(SLOTS):
                    n = unit + k
                    if expert is None:
                        s1, s3 = (w.rearrange("(k p) (s h) -> s p k h", p=P, h=H)[k] for w in (ws1, ws3))
                        s2 = ws2[k * H:(k + 1) * H, :]
                    else:
                        eng.wait_ge(w_split, n - SLOTS + 1)
                        s1, s3 = (w.rearrange("e (k p) h -> e p k h", p=P)[bass.ds(expert + k, 1)]
                                  .rearrange("e p k h -> (e p) k h") for w in (we1, we3))
                        s2 = we2[bass.ds(expert + k, 1)].rearrange("e h d -> (e h) d")
                    for m, s in enumerate((s1, s3)):
                        dst = w_raw[:, k, m * KD * H:(m + 1) * KD * H].rearrange("p (k h) -> p k h", k=KD)
                        eng.dma_start(dst, s).then_inc(w_in[k], 16)
                    eng.dma_start(w2(w_raw, k), s2).then_inc(w_in[k], 16)

            groups(load)(sp)
            for h in range(2):
                for j in range(2):
                    sp.wait_ge(added, 4 * (UNITS - 1) + 2 * h + j + 1)
                    t = TH * h + 2 * j
                    sp.dma_start(out_tiles[:, t:t + 2, :], acc[:, t:t + 2, :]).then_inc(out_done, 16)
            sp.wait_ge(out_done, 16 * 4)

        @block.gpsimd
        def _(pool):
            pool.iota(chan_i[:, :], pattern=[[-C, Q]], base=0, channel_multiplier=1).then_inc(iota_done, 1)
            pool.wait_ge(iota_done, 1)
            pool.iota(iota_i[:, :], pattern=[[1, E]], base=0, channel_multiplier=0).then_inc(iota_done, 1)
            pool.memset(ident[:, :], 1.0).then_inc(ident_done, 1)
            pool.wait_ge(ident_done, 1)
            pool.affine_select(out=ident[:, :], in_=ident[:, :], compare_op=ALU.is_equal, fill=0.0, base=0,
                               pattern=[[-1, 2 * E]], channel_multiplier=1).then_inc(ident_done, 1)
            pool.wait_ge(idx_done, Q)
            for t in range(TT):
                pool.indirect_dma_start(
                    cond_g[:, t, :], None, cond_rows,
                    bass.IndirectOffsetOnAxis(ap=gather_idx[:, t:t + 1], axis=0),
                ).then_inc(gathered[t // TH], 16)

            def split(eng, unit, expert):
                for k in range(LEAD if expert is None else 0, SLOTS):
                    n = unit + k
                    eng.wait_ge(w_in[k], 48 * ((unit + SLOTS) // SLOTS) if expert is None else (expert + 2 * SLOTS) * (48 // SLOTS))
                    if expert is not None:
                        eng.wait_ge(down_done, 4 * (n - SLOTS + 1))
                    lead = LEAD if expert is None and k == LEAD else 0
                    if lead:
                        eng.wait_ge(lead_split, LEAD)
                    eng.tensor_tensor(w_hi[:, k, :], w_raw[:, k, :], zeros[:, :], ALU.add).then_inc(w_hi_done, 1 + lead)
                    eng.wait_ge(w_hi_done, n + 1)
                    eng.tensor_tensor(w_lo[:, k, :], w_raw[:, k, :], w_hi[:, k, :].bitcast(F32), ALU.subtract).then_inc(w_split, 1 + lead)

            pool.wait_ge(bd_zero, 2)
            groups(split)(pool)

        @block.scalar
        def _(act):
            act.dma_start(wr[:, :, :], w_router.rearrange("(k p) e -> p k e", p=P)).then_inc(wr_in, 16)
            act.wait_ge(wr_in, 16)
            act.activation(wr_pair[:, :, 0, :], wr[:, :, :], ACT.Copy).then_inc(wr_hi_done, 1)
            for k in range(LEAD):
                act.wait_ge(w_in[k], 48)
                act.activation(w_hi[:, k, :], w_raw[:, k, :], ACT.Copy).then_inc(lead_hi, 1)

            def round_y(h):
                act.wait_ge(cond_done, h + 1)
                for k in range(KD):
                    act.activation(y_hi[:, k, h * HALF:(h + 1) * HALF], y_ps[h][k][:, :], ACT.Copy).then_inc(y_hi_done, 1)

            round_y(0)

            def activations(eng, unit, expert):
                for k in range(SLOTS):
                    for h in range(2):
                        s = (unit + k) * 2 + h
                        first = expert is None and k == 0
                        if expert is None and s == 1:
                            round_y(1)
                            for j in range(2):
                                eng.wait_ge(lgt_done, j + 1)
                                eng.activation(lgt[:, j * HALF:(j + 1) * HALF], lgt_ps[j], ACT.Copy).then_inc(lgt_out, 1)
                        if expert is None and s == EXP_STEP:
                            eng.wait_ge(exp_in, 1)
                            eng.activation(prob[:, :, :], lg[:, :, :], ACT.Exp).then_inc(exp_done, 1)
                        eng.wait_ge(gate_done, s + 1)
                        if not first:
                            eng.wait_ge(g_done, s - 1)
                        eng.activation(sil[:, h, :], gate_ps[h][:, :], ACT.Silu).then_inc(silu_done, 1)
                        eng.wait_ge(g_done, s + 1)
                        if not first:
                            eng.wait_ge(down_done, 2 * (s - 1))
                        eng.activation(g_hi[:, h, :], g[:, h, :], ACT.Copy).then_inc(g_hi_done, 1)

            groups(activations)(act)

        @block.vector
        def _(dve):
            dve.wait_ge(iota_done, 2)
            dve.tensor_copy(chan[:, :], chan_i[:, :]).then_inc(route, 1)
            dve.tensor_copy(iota_e[:, :], iota_i[:, :]).then_inc(route, 1)
            dve.wait_ge(route, 2)
            dve.wait_ge(itok_in, 16)
            for q in range(Q):
                r = slice(q * C, (q + 1) * C)
                dve.tensor_scalar(gather_idx[r, :], itok_all[r, q::Q], float(C), chan[r, q:q + 1], ALU.mult, ALU.add).then_inc(idx_done, 1)
            dve.memset(cond_bd[:, :, :], 0.0).then_inc(bd_zero, 1)
            dve.memset(zeros[:, :], 0.0).then_inc(bd_zero, 1)
            dve.memset(cw[:, 0:NSH, :], 1.0 / (TOP_K + 1)).then_inc(bd_zero, 1)
            dve.wait_ge(wr_hi_done, 1)
            dve.tensor_tensor(wr_pair[:, :, 1, :], wr[:, :, :], wr_pair[:, :, 0, :].bitcast(F32), ALU.subtract).then_inc(wr_lo_done, 1)
            dve.wait_ge(bd_zero, 3)

            def block_diagonal(h):
                dve.wait_ge(gathered[h], 16 * TH)
                for q in range(Q):
                    r = slice(q * C, (q + 1) * C)
                    t = slice(TH * h, TH * h + TH)
                    dve.tensor_copy(cond_bd[r, t, r], cond_g[r, t, :]).then_inc(bd_done, 1)

            def rest_of_y(h):
                for k in range(KD):
                    dve.wait_ge(y_hi_done, KD * h + k + 1)
                    r = slice(h * HALF, (h + 1) * HALF)
                    dve.tensor_tensor(y_lo[:, k, r], y_ps[h][k][:, :], y_hi[:, k, r].bitcast(F32), ALU.subtract).then_inc(y_lo_done, 1)

            def rest_of_lead(k):
                dve.wait_ge(lead_hi, k + 1)
                dve.tensor_tensor(w_lo[:, k, :], w_raw[:, k, :], w_hi[:, k, :].bitcast(F32), ALU.subtract).then_inc(lead_split, 1)

            rest_of_lead(0)
            block_diagonal(0)
            rest_of_y(0)
            block_diagonal(1)
            rest_of_lead(1)

            done = [2]

            def chain(ins):
                done[0] += 1
                ins.then_inc(route, 1)
                dve.wait_ge(route, done[0])

            def over_e(v):
                return v.rearrange("p (t a) -> p t a", a=1).to_broadcast((P, TT, E))

            lg_v = lg_ps[:, 0, 0:TT * 2 * E].rearrange("p (t m e) -> p t m e", e=E, m=2)
            iota_v = iota_e[:, :].rearrange("p (a e) -> p a e", a=1).to_broadcast((P, TT * TOP_K, E))

            def routing_logits():
                dve.wait_ge(lg_done, 1)
                chain(dve.tensor_copy(lg[:, :, :], lg_v[:, :, 0, :]))
                chain(dve.tensor_tensor(lg[:, :, :], lg_v[:, :, 1, :], lg[:, :, :], ALU.add))
                chain(dve.tensor_reduce(lmax[:, :], lg[:, :, :], AX.X, ALU.max))
                dve.tensor_tensor(lg[:, :, :], lg[:, :, :], over_e(lmax[:, :]), ALU.subtract).then_inc(exp_in, 1)

            def routing_softmax():
                dve.wait_ge(exp_done, 1)
                chain(dve.tensor_reduce(psumv[:, :], prob[:, :, :], AX.X, ALU.add))
                chain(dve.reciprocal(prec[:, :], psumv[:, :]))
                chain(dve.tensor_tensor(prob[:, :, :], prob[:, :, :], over_e(prec[:, :]), ALU.mult))

            def routing_top(tiles):
                for t in tiles:
                    dve.max(top_v[:, t, :], prob[:, t, :]).then_inc(route, 1)
                done[0] += len(tiles)
                dve.wait_ge(route, done[0])
                for t in tiles:
                    dve.max_index(top_i[:, t, :], top_v[:, t, :], prob[:, t, :]).then_inc(route, 1)
                done[0] += len(tiles)
                dve.wait_ge(route, done[0])

            def routing_masks():
                chain(dve.tensor_copy(top_f[:, :, :], top_i[:, :, 0:TOP_K]))
                chain(dve.tensor_tensor(pick[:, :, :, :].rearrange("p t k e -> p (t k) e"), iota_v,
                                        top_f[:, :, :].rearrange("p t (k a) -> p (t k) a", a=1).to_broadcast((P, TT * TOP_K, E)),
                                        ALU.is_equal))
                chain(dve.tensor_reduce(mask[:, :, :], pick[:, :, :, :].rearrange("p t k e -> p t e k"), AX.X, ALU.add))

            def routing_weights():
                chain(dve.tensor_reduce(top_s[:, :], top_v[:, :, 0:TOP_K], AX.X, ALU.add))
                chain(dve.reciprocal(top_r[:, :], top_s[:, :]))
                chain(dve.tensor_scalar(top_r[:, :], top_r[:, :], TOP_K / (TOP_K + 1.0), None, ALU.mult))
                chain(dve.tensor_tensor(mask[:, :, :], mask[:, :, :], prob[:, :, :], ALU.mult))
                chain(dve.tensor_tensor(cw[:, NSH:UNITS, :].rearrange("p e t -> p t e"), mask[:, :, :], over_e(top_r[:, :]), ALU.mult))

            routing = {1: routing_logits, EXP_STEP: routing_softmax,
                       EXP_STEP + 1: lambda: routing_top(range(TH)),
                       EXP_STEP + 2: lambda: routing_top(range(TH, TT)),
                       EXP_STEP + 3: routing_masks, EXP_STEP + 4: routing_weights}
            assert EXP_STEP + 4 < 2 * NSH

            def add(eng, n, h, j):
                eng.wait_ge(down_done, 2 * (n * 2 + h) + j + 1)
                for i in range(2):
                    t = TH * h + 2 * j + i
                    scale = cw[:, bass.ds(n, 1), t:t + 1].rearrange("p a b -> p (a b)")
                    ins = eng.scalar_tensor_tensor(out=acc[:, t, :], in0=down_ps[h][j][:, i, :], scalar=scale,
                                                   in1=acc[:, t, :], op0=ALU.mult, op1=ALU.add)
                ins.then_inc(added, 1)

            def gates(eng, unit, expert):
                for k in range(SLOTS):
                    for h in range(2):
                        s = (unit + k) * 2 + h
                        static = expert is None
                        if static and s == 1:
                            rest_of_y(1)
                        eng.wait_ge(silu_done, s + 1)
                        eng.wait_ge(up_done, s + 1)
                        if not static or k > 0:
                            eng.wait_ge(g_hi_done, s - 1)
                            eng.wait_ge(g_lo_done, s - 1)
                        eng.tensor_tensor(g[:, h, :], sil[:, h, :], up_ps[h][:, :], ALU.mult).then_inc(g_done, 1)
                        before = (unit + k, 0) if h else (unit + k - 1, 1)
                        has_before = h or k or not static
                        if has_before:
                            add(eng, *before, 0)
                        eng.wait_ge(g_hi_done, s + 1)
                        if not static or k > 0:
                            eng.wait_ge(down_done, 2 * (s - 1))
                        eng.tensor_tensor(g_lo[:, h, :], g[:, h, :], g_hi[:, h, :].bitcast(F32), ALU.subtract).then_inc(g_lo_done, 1)
                        if has_before:
                            add(eng, *before, 1)
                        if static and s in routing:
                            routing[s]()
            groups(gates)(dve)
            for j in range(2):
                add(dve, UNITS - 1, 1, j)

        @block.tensor
        def _(pe):
            def condition(h):
                pe.wait_ge(x_in[h], 16)
                pe.wait_ge(bd_done, Q * (h + 1))
                for t in range(TH * h, TH * h + TH):
                    for k in range(KD):
                        c = (t % TH) * P
                        last = pe.matmul(y_ps[h][k][:, c:c + P], acc[:, t, k * P:(k + 1) * P], cond_bd[:, t, :],
                                         start=True, stop=True)
                last.then_inc(cond_done, 1)

            def logits(h):
                n = 0
                for k in range(KD):
                    for y in (y_hi, y_lo):
                        last = pe.matmul(lgt_ps[h], wr_pair[:, k, :, :].rearrange("p m e -> p (m e)"), y[:, k, h * HALF:(h + 1) * HALF],
                                         start=(n == 0), stop=(n == 2 * KD - 1))
                        n += 1
                last.then_inc(lgt_done, 1)

            def turn_logits():
                pe.wait_ge(lgt_out, 2)
                for t in range(TT):
                    last = pe.transpose(lg_ps[:, 0, t * 2 * E:(t + 1) * 2 * E], lgt[:, t * P:(t + 1) * P], ident[:, :])
                last.then_inc(lg_done, 1)

            def down(eng, n, k, h, first):
                s = n * 2 + h
                eng.wait_ge(g_hi_done, s + 1)
                eng.wait_ge(g_lo_done, s + 1)
                if first and h:
                    eng.wait_ge(exp_in, 1)
                for j in range(2):
                    if not first:
                        eng.wait_ge(added, 2 * (s - 2) + j + 1)
                    for i in range(2):
                        c = (2 * j + i) * P
                        for m, (a, b) in enumerate([(g_hi, w_hi), (g_hi, w_lo), (g_lo, w_hi)]):
                            last = eng.matmul(down_ps[h][j][:, i, :], a[:, h, c:c + P], w2(b, k), start=(m == 0), stop=(m == 2))
                    last.then_inc(down_done, 1)

            def products(eng, unit, expert):
                for k in range(SLOTS):
                    static = expert is None
                    if static and k < LEAD:
                        if k:
                            eng.wait_ge(lead_split, k + 1)
                    else:
                        eng.wait_ge(w_split, unit + k + 1)
                    for h in range(2):
                        s = (unit + k) * 2 + h
                        first = static and k == 0
                        if first:
                            condition(h)
                            if h:
                                eng.wait_ge(wr_hi_done, 1)
                                eng.wait_ge(wr_lo_done, 1)
                                logits(0)
                            eng.wait_ge(y_hi_done, KD * (h + 1))
                            eng.wait_ge(y_lo_done, KD * (h + 1))
                            if h:
                                logits(1)
                            else:
                                eng.wait_ge(lead_split, 1)
                        for m, (ps, free, ready) in enumerate([(gate_ps, silu_done, gate_done), (up_ps, g_done, up_done)]):
                            if not first:
                                eng.wait_ge(free, s - 1)
                            n = 0
                            for kd in range(KD):
                                for a, b in [(w_hi, y_hi), (w_hi, y_lo), (w_lo, y_hi)]:
                                    last = eng.matmul(ps[h][:, :], w13(a, k, m, kd), b[:, kd, h * HALF:(h + 1) * HALF],
                                                      start=(n == 0), stop=(n == 3 * KD - 1))
                                    n += 1
                            last.then_inc(ready, 1)
                        if first and h:
                            pe.wait_ge(ident_done, 2)
                            turn_logits()
                        if h:
                            down(eng, unit + k, k, 0, first)
                        elif k or not static:
                            down(eng, unit + k - 1, (k - 1) % SLOTS, 1, static and k == 1)

            groups(products)(pe)
            down(pe, UNITS - 1, SLOTS - 1, 1, False)

    return nc


_INS = ["x", "itok_B_1_198", "L0_cond_weights", "L0_ffn_w_router", "L0_ffn_we1", "L0_ffn_we3", "L0_ffn_we2",
        "L0_ffn_ws1", "L0_ffn_ws3", "L0_ffn_ws2"]


def kernel(**inputs):
    import concourse.bacc as bacc
    from concourse.bass_utils import run_bass_kernel_spmd

    nc = bacc.Bacc("TRN2", target_bir_lowering=False, num_devices=1)
    arrays, args = {}, []
    for name in _INS:
        a = np.ascontiguousarray(inputs[name])
        arrays[f"in_{name}"] = a
        args.append(nc.dram_tensor(f"in_{name}", a.shape, mybir.dt.from_np(a.dtype), kind="ExternalInput").ap())
    out = nc.dram_tensor("out", inputs["x"].shape, F32, kind="ExternalOutput").ap()
    adaln_ffn(nc, *args, out)
    return run_bass_kernel_spmd(nc, [arrays], core_ids=[0]).results[0]["out"]
```

```python
from contextlib import ExitStack

import numpy as np

import concourse.bass as bass
from concourse import mybir

ALU = mybir.AluOpType
ACT = mybir.ActivationFunctionType
AX = mybir.AxisListType
F32 = mybir.dt.float32
BF16 = mybir.dt.bfloat16
F32R = mybir.dt.float32r
I32 = mybir.dt.int32
U32 = mybir.dt.uint32

P = 128
TOP_K = 4


def adaln_ffn(nc, x, itok, cond_w, w_router, we1, we3, we2, ws1, ws3, ws2, out):
    B, C, D = x.shape
    E, _, H = we1.shape
    HS = ws1.shape[1]
    T = B * C
    KD = D // P
    TT = T // P
    Q = P // C
    HALF = T // 2
    TH = HALF // P
    NSH = HS // H
    UNITS = NSH + E
    WC = 2 * KD * H + D
    RAW = 4
    LEAD = 2
    POOL_E = 2
    ROUNDED = [1, 1, 1, 2, 2, 2, 2, 3]
    AMID = [0, 1, 1, 1, 1, 1, 1, 1]
    BEHIND = [0, 0, 0, 1, 1, 1, 1, 0]
    LAST = 3
    POOL_TILES = (5,)
    WARM = 8
    STAY_WARM = 7
    TILES = T * TOP_K // P
    ITEMS = TILES + E - 1
    PAIRS = (ITEMS + 1) // 2
    ITEMS_UP = 2 * PAIRS
    XW = D + 2
    RESULTS = T * TOP_K
    KEY = 2 * RESULTS
    RING = 4
    LAG = 2
    assert POOL_E + sum(ROUNDED) == E and POOL_E + sum(AMID) + sum(BEHIND) + LAST == E
    assert KEY & (KEY - 1) == 0 and NSH == RAW and E % RAW == 0 and H == P and D == 2 * H and HALF == 512 and TH == 4

    with ExitStack() as ctx:
        def sb(name, shape, dt=F32):
            return ctx.enter_context(nc.sbuf_tensor(name, shape, dt))

        def sem(name):
            return ctx.enter_context(nc.semaphore(name))

        sent = nc.dram_tensor("sent", [RESULTS, XW], F32).ap()
        result = nc.dram_tensor("result", [RESULTS, D], F32).ap()

        acc = sb("acc", [P, TT, D])
        itok_all = sb("itok_all", [P, B], I32)
        chan = sb("chan", [P, Q])
        chan_i = sb("chan_i", [P, Q], I32)
        gather_idx = sb("gather_idx", [P, TT], I32)
        cond_g = sb("cond_g", [P, TT, C])
        cond_bd = sb("cond_bd", [P, TT, P])
        y_hi = sb("y_hi", [P, KD, T], F32R)
        y_lo = sb("y_lo", [P, KD, T], F32R)
        rows = sb("rows", [P, 2 * TT * XW])
        y_row = rows[:, :].rearrange("p (c t w) -> p c t w", c=2, w=XW)
        where_i = sb("where_i", [P, TT, TOP_K], I32)
        where = sb("where", [P, TT, TOP_K])
        key = sb("key", [P, TT, TOP_K])
        wr = sb("wr", [P, KD, E])
        wr_pair = sb("wr_pair", [P, KD, 2, E], F32R)
        lgt = sb("lgt", [2 * E, T])
        ident = sb("ident", [P, P])
        w_raw = sb("w_raw", [P, RAW, WC])
        w_hi = sb("w_hi", [P, E, WC], F32R)
        w_lo = sb("w_lo", [P, E, WC], F32R)
        back_in = w_lo[:, :, :].rearrange("p e n -> p (e n)")[:, 0:TT * TOP_K * D].bitcast(F32).rearrange(
            "p (t k d) -> p t k d", t=TT, k=TOP_K)
        pair_sums = rows[:, 0:TT * 2 * D].rearrange("p (t k d) -> p t k d", t=TT, k=2)
        sil = sb("sil", [P, 2, HALF])
        g = sb("g", [P, 2, HALF])
        g_hi = sb("g_hi", [P, 2, HALF], F32R)
        g_lo = sb("g_lo", [P, 2, HALF], F32R)
        xt = sb("xt", [P, RING, 2, XW])
        yo = sb("yo", [P, RING, 2, D])
        zeros = xt[:, :, :, :].rearrange("p r i w -> p (r i w)")[:, 0:WC]
        warm = yo[:, 0, :, :].rearrange("p i d -> p (i d)")
        dest_i = sb("dest_i", [P, PAIRS, 2], I32)
        lg = sb("lg", [P, TT, E])
        lmax = sb("lmax", [P, TT])
        prob = sb("prob", [P, TT, E])
        psumv = sb("psumv", [P, TT])
        prec = sb("prec", [P, TT])
        top_v = sb("top_v", [P, TT, 8])
        top_i = sb("top_i", [P, TT, 8], U32)
        top_f = sb("top_f", [P, TT, TOP_K])
        top_w = sb("top_w", [P, TT, TOP_K])
        top_s = sb("top_s", [P, TT])
        top_r = sb("top_r", [P, TT])
        iota_i = sb("iota_i", [P, E], I32)
        iota_e = sb("iota_e", [P, E])
        pick = sb("pick", [P, TT, TOP_K, E])
        picked = sb("picked", [P, TT, TOP_K, E])
        mask = sb("mask", [P, TT, E], BF16)
        tri = sb("tri", [P, P], BF16)
        ones = sb("ones", [P, P], BF16)
        tri_e = sb("tri_e", [P, E, E])
        count = sb("count", [P, E])
        before_e = sb("before_e", [P, E, E])
        base_e = sb("base_e", [P, E])
        end_e = sb("end_e", [P, E])
        span_i = sb("span_i", [P, 2, E], I32)
        span = sb("span", [P, 2, E])
        spanned = sb("spanned", [P, E])
        base_i = sb("base_i", [P, E])
        end_i = sb("end_i", [P, E])
        ahead = sb("ahead", [P, E])
        stride = sb("stride", [P, E])
        slot_te = sb("slot_te", [P, TT, E])
        slot_i = sb("slot_i", [P, TT, TOP_K], I32)
        item_i = sb("item_i", [P, ITEMS_UP], I32)
        item = sb("item", [P, ITEMS_UP])
        ended = sb("ended", [P, ITEMS_UP, E])
        item_e = sb("item_e", [P, ITEMS_UP])
        item_key = sb("item_key", [P, PAIRS, 2], I32)
        item_t = sb("item_t", [P, ITEMS_UP])
        row_w = sb("row_w", [P, RING, 2])
        item_e_i = sb("item_e_i", [1, PAIRS + 1, 4], I32)
        item_t_i = sb("item_t_i", [1, ITEMS_UP], I32)

        gate_ps = [ctx.enter_context(nc.psum_tensor(f"gate_ps{h}", [P, HALF], F32)) for h in range(2)]
        up_ps = [ctx.enter_context(nc.psum_tensor(f"up_ps{h}", [P, HALF], F32)) for h in range(2)]
        down_ps = [[ctx.enter_context(nc.psum_tensor(f"down_ps{h}{j}", [P, HALF], F32)) for j in range(2)]
                   for h in range(2)]
        y_ps = [[gate_ps[h], up_ps[h]] for h in range(2)]
        lgt_ps = [down_ps[1][j][0:2 * E, :] for j in range(2)]
        lg_ps = down_ps[1][1]
        rank_ps = down_ps[1][1]
        row_ps = [down_ps[0][0], down_ps[0][1], gate_ps[1], up_ps[1]]
        xt_ps, gu_ps, out_ps = ([b[:, :].rearrange("p (i d) -> p i d", i=2) for b in banks] for banks in (gate_ps, up_ps, down_ps[1]))
        gt_ps = [b[:, 0:2 * P].rearrange("p (i d) -> p i d", i=2) for b in down_ps[0]]
        tx = [y[:, :, 0:HALF].rearrange("p b (i d) -> p b i d", i=2) for y in (y_hi, y_lo)]
        tg = [v[:, :, 0:2 * P].rearrange("p b (i d) -> p b i d", i=2) for v in (g_hi, g_lo)]
        t_sil, t_gated = (v[:, :, 0:2 * P].rearrange("p b (i d) -> p b i d", i=2) for v in (sil, g))

        x_in = [sem(f"x_in{h}") for h in range(2)]
        itok_in = sem("itok_in")
        wr_in = sem("wr_in")
        iota_done = sem("iota_done")
        const_done = sem("const_done")
        idx_done = sem("idx_done")
        gathered = [sem(f"gathered{h}") for h in range(2)]
        zeroed = sem("zeroed")
        bd_done = sem("bd_done")
        warm_ready = sem("warm_ready")
        cond_done = sem("cond_done")
        y_hi_done = sem("y_hi_done")
        y_lo_done = sem("y_lo_done")
        wr_hi_done = sem("wr_hi_done")
        wr_lo_done = sem("wr_lo_done")
        lgt_done = sem("lgt_done")
        lgt_out = sem("lgt_out")
        lg_done = sem("lg_done")
        row_done = sem("row_done")
        row_out = sem("row_out")
        key_done = sem("key_done")
        route = sem("route")
        exp_in = sem("exp_in")
        exp_done = sem("exp_done")
        mask_done = sem("mask_done")
        rank_done = sem("rank_done")
        slot_done = sem("slot_done")
        items_done = sem("items_done")
        token_sent = [sem(f"token_sent{k}") for k in range(TOP_K)]
        w_in = [sem(f"w_in{k}") for k in range(RAW)]
        lead_hi = sem("lead_hi")
        lead_split = sem("lead_split")
        pool_hi = sem("pool_hi")
        pool_split = sem("pool_split")
        late_hi = sem("late_hi")
        late_split = sem("late_split")
        gate_done = sem("gate_done")
        up_done = sem("up_done")
        silu_done = sem("silu_done")
        g_done = sem("g_done")
        g_hi_done = sem("g_hi_done")
        g_lo_done = sem("g_lo_done")
        down_done = sem("down_done")
        added = sem("added")
        xt_in = [sem(f"xt_in{r}") for r in range(RING)]
        t_turned = sem("t_turned")
        t_x_hi = sem("t_x_hi")
        t_x_lo = sem("t_x_lo")
        t_dest = sem("t_dest")
        t_weight = sem("t_weight")
        t_gate_up = sem("t_gate_up")
        t_silu = sem("t_silu")
        t_g = sem("t_g")
        t_g_turned = sem("t_g_turned")
        t_g_hi = sem("t_g_hi")
        t_g_lo = sem("t_g_lo")
        t_down = sem("t_down")
        t_out = sem("t_out")
        result_out = [sem(f"result_out{r}") for r in range(RING)]
        back = [sem(f"back{t}") for t in range(TT)]
        combined = [sem(f"combined{t}") for t in range(TT)]
        out_done = sem("out_done")

        x_tiles = x.rearrange("(g q) c t -> (q c) g t", q=Q)
        out_tiles = out.rearrange("(g q) c t -> (q c) g t", q=Q)
        cond_rows = cond_w.rearrange("s c d -> (s c) d")

        def w_slot(u):
            return E - NSH + u

        def w13(w, slot, m, k):
            at = (k * 2 + m) * H
            return w[:, slot, at:at + H]

        def w2(w, slot):
            return w[:, slot, 2 * KD * H:WC]

        def of(w, e, a, b):
            return w[:, bass.ds(e, 1), a:b].rearrange("p a n -> p (a n)")

        def spread(v, n):
            return v.rearrange("p (a b) -> p a b", b=1).to_broadcast((v.shape[0], v.shape[1], n))

        def repeat(v, n):
            return v.rearrange("p (b a) -> p b a", b=1).to_broadcast((v.shape[0], n, v.shape[1]))

        START = LAG + RING
        LOOPS = (PAIRS - START) // RING

        def rounds(eng, body):
            def at(q, r):
                def pair(d):
                    a, b = (q, r - d) if r >= d else (q - 1, r - d + RING)
                    if isinstance(q, int) and not 0 <= RING * a + b < PAIRS:
                        return None
                    return a, b
                body(pair)

            for i in range(START):
                at(i // RING, i % RING)
            with eng.Fori(0, LOOPS) as m:
                for u in range(RING):
                    at(m + (START + u) // RING, (START + u) % RING)
            for i in range(START + LOOPS * RING, PAIRS + LAG):
                at(i // RING, i % RING)

        def number(pair):
            return RING * pair[0] + pair[1]

        def halves(n):
            return 1 if ITEMS % 2 and isinstance(n, int) and n == PAIRS - 1 else 2

        def reused(pair):
            return not isinstance(pair[0], int) or pair[0] > 0

        def combine(eng, t):
            half = pair_sums[:, t, :, :]
            eng.wait_ge(back[t], 16)
            eng.tensor_tensor(half, back_in[:, t, 0:2, :], back_in[:, t, 2:4, :], ALU.add).then_inc(combined[t], 1)
            eng.wait_ge(combined[t], 1)
            eng.tensor_tensor(half[:, 0, :], half[:, 0, :], half[:, 1, :], ALU.add).then_inc(combined[t], 1)
            eng.wait_ge(combined[t], 2)
            eng.tensor_tensor(acc[:, t, :], acc[:, t, :], half[:, 0, :], ALU.add).then_inc(combined[t], 1)

        def store(eng, t):
            eng.wait_ge(combined[t], 3)
            eng.dma_start(out_tiles[:, t, :], acc[:, t, :]).then_inc(out_done, 16)

        block = ctx.enter_context(nc.Block())

        @block.sync
        def _(sp):
            sp.dma_start(itok_all[:, :], itok.rearrange("(a b) -> a b", a=1).to_broadcast((P, B))).then_inc(itok_in, 16)
            for h in range(2):
                sp.dma_start(acc[:, TH * h:TH * h + TH, :], x_tiles[:, TH * h:TH * h + TH, :]).then_inc(x_in[h], 16)

            def load(k, s1, s3, s2):
                for m, s in enumerate((s1, s3)):
                    dst = w_raw[:, k, 0:2 * KD * H].rearrange("p (k m h) -> p k m h", k=KD, m=2)[:, :, m, :]
                    sp.dma_start(dst, s).then_inc(w_in[k], 16)
                sp.dma_start(w2(w_raw, k), s2).then_inc(w_in[k], 16)

            def load_expert(k, e):
                s1, s3 = (w.rearrange("e (k p) h -> e p k h", p=P)[bass.ds(e, 1)]
                          .rearrange("e p k h -> (e p) k h") for w in (we1, we3))
                load(k, s1, s3, we2[bass.ds(e, 1)].rearrange("e h d -> (e h) d"))

            for k in range(NSH):
                s1, s3 = (w.rearrange("(k p) (s h) -> s p k h", p=P, h=H)[k] for w in (ws1, ws3))
                load(k, s1, s3, ws2[k * H:(k + 1) * H, :])
            for k in range(RAW):
                if k < LEAD:
                    sp.wait_ge(lead_split, k + 1)
                else:
                    sp.wait_ge(pool_split, k - LEAD + 1)
                load_expert(k, k)
            for k in range(POOL_E):
                sp.wait_ge(pool_split, NSH - LEAD + k + 1)
                load_expert(k, RAW + k)
            for k in range(POOL_E, RAW):
                sp.wait_ge(late_split, k - POOL_E + 1)
                load_expert(k, RAW + k)
            with sp.Fori(2, E // RAW) as i:
                for k in range(RAW):
                    sp.wait_ge(late_split, (i - 1) * RAW + k - POOL_E + 1)
                    load_expert(k, i * RAW + k)

            sp.wait_ge(items_done, 5)
            loads = []

            def load_tiles(n):
                registers = [sp.alloc_register(f"tile{len(loads)}_{i}") for i in range(2)]
                loads.append(n)
                sp.load(registers, item_t_i[0:1, bass.ds(2 * n, 2)])
                return [sp.snap(r, donate=True, min_val=0, max_val=TILES - 1) for r in registers]

            def load_pair(pair):
                t = pair(0)
                if t is None:
                    return
                tiles = load_tiles(number(t))
                if isinstance(t[0], int) and t == (0, 0):
                    for k in range(TOP_K):
                        sp.wait_ge(token_sent[k], 16 * TT)
                if reused(t):
                    sp.wait_ge(t_dest, number(t) - RING + 1)
                for i in range(2):
                    src = sent.rearrange("(t p) w -> t p w", p=P)[bass.ds(tiles[i], 1)].rearrange("t p w -> (t p) w")
                    sp.dma_start(xt[:, t[1], i, :], src).then_inc(xt_in[t[1]], 16)

            rounds(sp, load_pair)

            for r in range(RING):
                sp.wait_ge(result_out[r], 16 * sum(halves(n) for n in range(r, PAIRS, RING)))
            for t in range(TT):
                src = result.rearrange("(t p k) d -> t p (k d)", p=P, k=TOP_K)[t]
                sp.dma_start(back_in[:, t, :, :].rearrange("p k d -> p (k d)"), src).then_inc(back[t], 16)
            for t in POOL_TILES:
                store(sp, t)

        @block.gpsimd
        def _(pool):
            pool.iota(chan_i[:, :], pattern=[[-C, Q]], base=0, channel_multiplier=1).then_inc(iota_done, 1)
            pool.iota(iota_i[:, :], pattern=[[1, E]], base=0, channel_multiplier=0).then_inc(const_done, 1)
            pool.iota(item_i[:, :], pattern=[[1, ITEMS_UP]], base=0, channel_multiplier=0).then_inc(const_done, 1)
            pool.iota(where_i[:, :, :], pattern=[[TOP_K * P, TT], [1, TOP_K]], base=0, channel_multiplier=TOP_K).then_inc(const_done, 1)
            pool.memset(ident[:, :], 1.0).then_inc(const_done, 1)
            pool.memset(tri[:, :], 1.0).then_inc(const_done, 1)
            pool.memset(tri_e[:, :, :], 1.0).then_inc(const_done, 1)
            pool.memset(ones[:, :], 1.0).then_inc(const_done, 1)
            pool.wait_ge(const_done, 7)
            pool.affine_select(out=ident[:, :], in_=ident[:, :], compare_op=ALU.is_equal, fill=0.0, base=0,
                               pattern=[[-1, P]], channel_multiplier=1).then_inc(const_done, 1)
            pool.affine_select(out=tri[:, :], in_=tri[:, :], compare_op=ALU.is_gt, fill=0.0, base=0,
                               pattern=[[1, P]], channel_multiplier=-1).then_inc(const_done, 1)
            pool.affine_select(out=tri_e[:, :, :], in_=tri_e[:, :, :], compare_op=ALU.is_gt, fill=0.0, base=0,
                               pattern=[[1, E], [-1, E]], channel_multiplier=0).then_inc(const_done, 1)
            pool.wait_ge(idx_done, Q)
            for t in range(TT):
                pool.indirect_dma_start(
                    cond_g[:, t, :], None, cond_rows,
                    bass.IndirectOffsetOnAxis(ap=gather_idx[:, t:t + 1], axis=0),
                ).then_inc(gathered[t // TH], 16)

            pool.wait_ge(zeroed, 2)
            for n in range(NSH - LEAD + POOL_E):
                k, use, slot = (n + LEAD, 1, w_slot(n + LEAD)) if n < NSH - LEAD else (n + LEAD - NSH, 2, n + LEAD - NSH)
                pool.wait_ge(w_in[k], 48 * use)
                pool.tensor_tensor(w_hi[:, slot, :], w_raw[:, k, :], zeros, ALU.add).then_inc(pool_hi, 1)
                pool.wait_ge(pool_hi, n + 1)
                pool.tensor_tensor(w_lo[:, slot, :], w_raw[:, k, :], w_hi[:, slot, :].bitcast(F32), ALU.subtract).then_inc(pool_split, 1)

            pool.wait_ge(key_done, 2)
            pool.wait_ge(row_out, 8)
            pool.wait_ge(slot_done, 1)
            for k in range(TOP_K):
                if k >= 2:
                    pool.wait_ge(token_sent[k - 2], 16 * TT)
                    pool.tensor_copy(y_row[:, k % 2, :, D].bitcast(I32), key[:, :, k]).then_inc(key_done, 1)
                    pool.tensor_copy(y_row[:, k % 2, :, D + 1], top_w[:, :, k]).then_inc(key_done, 1)
                    pool.wait_ge(key_done, 2 * k)
                for t in range(TT):
                    if k == 0 and t == TH:
                        pool.wait_ge(slot_done, 2)
                    pool.indirect_dma_start(
                        sent, bass.IndirectOffsetOnAxis(ap=slot_i[:, t, k:k + 1], axis=0),
                        y_row[:, k % 2, t, :], None,
                    ).then_inc(token_sent[k], 16)

            for n in range(PAIRS):
                r = n % RING
                pool.wait_ge(t_dest, n + 1)
                for i in range(halves(n)):
                    pool.wait_ge(t_out, 2 * n + i + 1)
                    pool.indirect_dma_start(
                        result, bass.IndirectOffsetOnAxis(ap=dest_i[:, n, i:i + 1], axis=0),
                        yo[:, r, i, :], None, bounds_check=RESULTS - 1, oob_is_err=False,
                    ).then_inc(result_out[r], 16)

            for t in POOL_TILES:
                combine(pool, t)

        @block.scalar
        def _(act):
            act.dma_start(wr[:, :, :], w_router.rearrange("(k p) e -> p k e", p=P)).then_inc(wr_in, 16)
            act.wait_ge(wr_in, 16)
            act.activation(wr_pair[:, :, 0, :], wr[:, :, :], ACT.Copy).then_inc(wr_hi_done, 1)

            def lead(k):
                act.wait_ge(w_in[k], 48)
                act.activation(w_hi[:, w_slot(k), :], w_raw[:, k, :], ACT.Copy).then_inc(lead_hi, 1)

            lead(0)
            lead(1)
            for h in range(2):
                for k in range(KD):
                    act.wait_ge(cond_done, KD * h + k + 1)
                    act.activation(y_hi[:, k, h * HALF:(h + 1) * HALF], y_ps[h][k][:, :], ACT.Copy).then_inc(y_hi_done, 1)
            for h in range(2):
                act.wait_ge(lgt_done, h + 1)
                act.activation(lgt[:, h * HALF:(h + 1) * HALF], lgt_ps[h], ACT.Copy).then_inc(lgt_out, 1)

            def copy_rows(j):
                act.wait_ge(row_done, j + 1)
                for c in range(2):
                    act.activation(y_row[:, c, 2 * j:2 * j + 2, 0:D], row_ps[j][:, :].rearrange("p (i d) -> p i d", i=2), ACT.Copy).then_inc(row_out, 1)

            copy_rows(0)
            act.wait_ge(exp_in, 1)
            act.activation(prob[:, :, :], lg[:, :, :], ACT.Exp).then_inc(exp_done, 1)
            for j in range(1, 4):
                copy_rows(j)

            def late(e):
                act.wait_ge(w_in[e % RAW], 48 * (e // RAW + 2))
                if e >= w_slot(0):
                    act.wait_ge(down_done, 2 * (e - w_slot(0) + 1))
                act.activation(w_hi[:, e, :], w_raw[:, e % RAW, :], ACT.Copy).then_inc(late_hi, 1)

            for s in range(2 * NSH):
                h = s % 2
                act.wait_ge(gate_done, s + 1)
                if s >= 2:
                    act.wait_ge(g_done, s - 1)
                act.activation(sil[:, h, :], gate_ps[h][:, :], ACT.Silu).then_inc(silu_done, 1)
                act.wait_ge(g_done, s + 1)
                if s >= 2:
                    act.wait_ge(down_done, s - 1)
                act.activation(g_hi[:, h, :], g[:, h, :], ACT.Copy).then_inc(g_hi_done, 1)
                first = POOL_E + sum(ROUNDED[:s])
                for e in range(first, first + ROUNDED[s]):
                    late(e)

            def pair_round(pair):
                if t := pair(2):
                    n, b, m = number(t), t[1] % 2, halves(number(t))
                    act.wait_ge(t_g_turned, n + 1)
                    act.activation(tg[0][:, b, 0:m, :], gt_ps[b][:, 0:m, :], ACT.Copy).then_inc(t_g_hi, 1)
                if t := pair(0):
                    n, b, m = number(t), t[1] % 2, halves(number(t))
                    act.wait_ge(t_turned, n + 1)
                    act.activation(tx[0][:, b, 0:m, :], xt_ps[b][:, 0:m, :], ACT.Copy).then_inc(t_x_hi, 1)
                if t := pair(1):
                    n, b, m = number(t), t[1] % 2, halves(number(t))
                    act.wait_ge(t_gate_up, n + 1)
                    act.activation(t_sil[:, b, 0:m, :], gu_ps[b][:, 0:m, 0:H], ACT.Silu).then_inc(t_silu, 1)
                if t := pair(2):
                    n, m = number(t), halves(number(t))
                    if reused(t):
                        act.wait_ge(result_out[t[1]], 32 * t[0])
                    act.wait_ge(t_down, n + 1)
                    act.wait_ge(t_weight, n + 1)
                    for i in range(m):
                        act.activation(yo[:, t[1], i, :], out_ps[t[1] % 2][:, i, :], ACT.Copy, scale=row_w[:, t[1], i:i + 1]).then_inc(t_out, 1)

            act.wait_ge(late_split, E - POOL_E)
            rounds(act, pair_round)

            for t in range(TT):
                if t not in POOL_TILES:
                    store(act, t)
            act.wait_ge(out_done, 16 * TT)

        @block.vector
        def _(dve):
            dve.memset(warm, 0.0).then_inc(warm_ready, 1)
            dve.wait_ge(iota_done, 1)
            dve.tensor_copy(chan[:, :], chan_i[:, :]).then_inc(route, 1)
            dve.wait_ge(route, 1)
            dve.wait_ge(itok_in, 16)
            for q in range(Q):
                r = slice(q * C, (q + 1) * C)
                dve.tensor_scalar(gather_idx[r, :], itok_all[r, q::Q], float(C), chan[r, q:q + 1], ALU.mult, ALU.add).then_inc(idx_done, 1)
            dve.memset(cond_bd[:, :, :], 0.0).then_inc(zeroed, 1)
            dve.memset(zeros, 0.0).then_inc(zeroed, 1)
            dve.memset(item_e_i[:, :, :], 0).then_inc(zeroed, 1)
            dve.wait_ge(wr_hi_done, 1)
            dve.tensor_tensor(wr_pair[:, :, 1, :], wr[:, :, :], wr_pair[:, :, 0, :].bitcast(F32), ALU.subtract).then_inc(wr_lo_done, 1)
            dve.wait_ge(zeroed, 3)

            def block_diagonal(h):
                dve.wait_ge(gathered[h], 16 * TH)
                for q in range(Q):
                    r = slice(q * C, (q + 1) * C)
                    t = slice(TH * h, TH * h + TH)
                    dve.tensor_copy(cond_bd[r, t, r], cond_g[r, t, :]).then_inc(bd_done, 1)

            def rest_of_lead(k):
                dve.wait_ge(lead_hi, k + 1)
                dve.tensor_tensor(w_lo[:, w_slot(k), :], w_raw[:, k, :], w_hi[:, w_slot(k), :].bitcast(F32), ALU.subtract).then_inc(lead_split, 1)

            rest_of_lead(0)
            block_diagonal(0)
            rest_of_lead(1)
            block_diagonal(1)
            for h in range(2):
                for k in range(KD):
                    dve.wait_ge(y_hi_done, KD * h + k + 1)
                    r = slice(h * HALF, (h + 1) * HALF)
                    dve.tensor_tensor(y_lo[:, k, r], y_ps[h][k][:, :], y_hi[:, k, r].bitcast(F32), ALU.subtract).then_inc(y_lo_done, 1)

            def gated(s):
                h = s % 2
                dve.wait_ge(silu_done, s + 1)
                dve.wait_ge(up_done, s + 1)
                if s >= 2:
                    dve.wait_ge(g_hi_done, s - 1)
                    dve.wait_ge(g_lo_done, s - 1)
                dve.tensor_tensor(g[:, h, :], sil[:, h, :], up_ps[h][:, :], ALU.mult).then_inc(g_done, 1)

            done = [1]

            def step(ins):
                done[0] += 1
                ins.then_inc(route, 1)

            def chain(ins):
                step(ins)
                dve.wait_ge(route, done[0])

            dve.wait_ge(const_done, 10)
            step(dve.tensor_copy(iota_e[:, :], iota_i[:, :]))
            step(dve.tensor_copy(where[:, :, :], where_i[:, :, :]))
            step(dve.tensor_copy(item[:, :], item_i[:, :]))
            dve.wait_ge(lg_done, 1)
            lg_v = lg_ps[:, 0:TT * 2 * E].rearrange("p (t m e) -> p t m e", e=E, m=2)
            chain(dve.tensor_reduce(lg[:, :, :], lg_v.rearrange("p t m e -> p t e m"), AX.X, ALU.add))
            chain(dve.tensor_reduce(lmax[:, :], lg[:, :, :], AX.X, ALU.max))
            dve.tensor_tensor(lg[:, :, :], lg[:, :, :], spread(lmax[:, :], E), ALU.subtract).then_inc(exp_in, 1)
            dve.wait_ge(exp_done, 1)
            chain(dve.tensor_reduce(psumv[:, :], prob[:, :, :], AX.X, ALU.add))
            chain(dve.reciprocal(prec[:, :], psumv[:, :]))
            chain(dve.tensor_tensor(prob[:, :, :], prob[:, :, :], spread(prec[:, :], E), ALU.mult))
            for t in range(TT):
                step(dve.max(top_v[:, t, :], prob[:, t, :]))
            dve.wait_ge(route, done[0])
            for t in range(TT):
                step(dve.max_index(top_i[:, t, :], top_v[:, t, :], prob[:, t, :]))
            found = done[0]
            step(dve.tensor_reduce(top_s[:, :], top_v[:, :, 0:TOP_K], AX.X, ALU.add))
            dve.wait_ge(route, found)
            step(dve.tensor_copy(top_f[:, :, :], top_i[:, :, 0:TOP_K]))
            dve.wait_ge(route, found + 1)
            step(dve.reciprocal(top_r[:, :], top_s[:, :]))
            dve.wait_ge(route, found + 2)
            step(dve.tensor_tensor(pick[:, :, :, :].rearrange("p t k e -> p (t k) e"), repeat(iota_e[:, :], TT * TOP_K),
                                   spread(top_f[:, :, :].rearrange("p t k -> p (t k)"), E), ALU.is_equal))
            dve.wait_ge(route, found + 3)
            step(dve.scalar_tensor_tensor(out=top_w[:, :, :], in0=top_v[:, :, 0:TOP_K], scalar=TOP_K / (TOP_K + 1.0),
                                          in1=spread(top_r[:, :], TOP_K), op0=ALU.mult, op1=ALU.mult))
            step(dve.scalar_tensor_tensor(out=key[:, :, :], in0=top_f[:, :, :], scalar=float(KEY), in1=where[:, :, :], op0=ALU.mult, op1=ALU.add))
            dve.wait_ge(route, found + 4)
            with nc.allow_low_precision(reason="0 and 1 are exact in bfloat16"):
                dve.tensor_reduce(mask[:, :, :], pick[:, :, :, :].rearrange("p t k e -> p t e k"), AX.X, ALU.add).then_inc(mask_done, 1)
            dve.wait_ge(route, found + 6)
            dve.tensor_copy(y_row[:, :, :, D].bitcast(I32), key[:, :, 0:2].rearrange("p t k -> p k t")).then_inc(key_done, 1)
            dve.tensor_copy(y_row[:, :, :, D + 1], top_w[:, :, 0:2].rearrange("p t k -> p k t")).then_inc(key_done, 1)
            dve.wait_ge(rank_done, 1)
            rank_v = rank_ps[:, 0:(TT + 1) * E].rearrange("p (t e) -> p t e", e=E)

            def before(out, v):
                chain(dve.tensor_tensor(before_e[:, :, :], tri_e[:, :, :], repeat(v, E), ALU.mult))
                chain(dve.tensor_reduce(out, before_e[:, :, :], AX.X, ALU.add))

            before(base_e[:, :], rank_v[:, TT, :])
            chain(dve.tensor_tensor(slot_te[:, :, :], repeat(base_e[:, :], TT), rank_v[:, 0:TT, :], ALU.add))
            for h in range(2):
                r = slice(TH * h, TH * h + TH)
                step(dve.tensor_tensor(picked[:, r, :, :], pick[:, r, :, :],
                                       slot_te[:, r, :].rearrange("p t (a e) -> p t a e", a=1).to_broadcast((P, TH, TOP_K, E)), ALU.mult))
                if h == 0:
                    step(dve.tensor_copy(count[:, :], rank_v[:, TT, :]))
                    dve.wait_ge(route, done[0] - 1)
                else:
                    dve.wait_ge(route, done[0])
                with nc.allow_low_precision(reason="whole numbers"):
                    dve.tensor_reduce(slot_i[:, r, :], picked[:, r, :, :], AX.X, ALU.add).then_inc(slot_done, 1)

            def spans():
                chain(dve.tensor_tensor(end_e[:, :], base_e[:, :], count[:, :], ALU.add))
                step(dve.tensor_copy(span_i[:, 0, :], base_e[:, :]))
                chain(dve.tensor_scalar(span_i[:, 1, :], end_e[:, :], float(P - 1), None, ALU.add))
                chain(dve.tensor_scalar(span_i[:, :, :], span_i[:, :, :], P.bit_length() - 1, None, ALU.logical_shift_right))
                chain(dve.tensor_copy(span[:, :, :], span_i[:, :, :]))
                chain(dve.tensor_tensor(spanned[:, :], span[:, 1, :], span[:, 0, :], ALU.subtract))
                chain(dve.scalar_tensor_tensor(out=count[:, :], in0=count[:, :], scalar=1.0, in1=spanned[:, :], op0=ALU.min, op1=ALU.mult))
                before(base_i[:, :], count[:, :])
                step(dve.tensor_tensor(end_i[:, :], base_i[:, :], count[:, :], ALU.add))
                step(dve.memset(stride[:, :], 0.0))
                chain(dve.tensor_tensor(ahead[:, :], span[:, 0, :], base_i[:, :], ALU.subtract))
                chain(dve.tensor_tensor(stride[:, 0:E - 1], ahead[:, 1:E], ahead[:, 0:E - 1], ALU.subtract))

            def experts_of_items():
                chain(dve.tensor_tensor(ended[:, :, :], repeat(end_i[:, :], ITEMS_UP), spread(item[:, :], E), ALU.is_le))
                chain(dve.tensor_reduce(item_e[:, :], ended[:, :, :], AX.X, ALU.add))
                pair_e = item_e[0:1, :].rearrange("p (n i) -> p n i", i=2)
                dve.tensor_scalar(item_e_i[:, 0:PAIRS, 0:2], pair_e, float(E - 1), None, ALU.min).then_inc(items_done, 1)
                dve.tensor_scalar(item_e_i[:, 1:PAIRS + 1, 2:4], pair_e, float(E - 1), None, ALU.min).then_inc(items_done, 1)
                dve.tensor_scalar(item_key[:, :, :], item_e[:, :].rearrange("p (n i) -> p n i", i=2), float(KEY), None,
                                  ALU.mult).then_inc(items_done, 1)

            def tiles_of_items():
                chain(dve.tensor_tensor(ended[:, :, :], ended[:, :, :], repeat(stride[:, :], ITEMS_UP), ALU.mult))
                chain(dve.tensor_reduce(item_t[:, :], ended[:, :, :], AX.X, ALU.add))
                dve.tensor_tensor(item_t[:, :], item_t[:, :], item[:, :], ALU.add).then_inc(items_done, 1)
                dve.wait_ge(items_done, 4)
                dve.tensor_scalar(item_t_i[:, :], item_t[0:1, :], float(TILES - 1), None, ALU.min).then_inc(items_done, 1)

            gated(0)

            def late(e):
                dve.wait_ge(late_hi, e - POOL_E + 1)
                dve.tensor_tensor(w_lo[:, e, :], w_raw[:, e % RAW, :], w_hi[:, e, :].bitcast(F32), ALU.subtract).then_inc(late_split, 1)

            for s in range(2 * NSH):
                h = s % 2
                if s:
                    gated(s)
                first = POOL_E + sum(AMID[:s]) + sum(BEHIND[:s])
                for e in range(first, first + AMID[s]):
                    late(e)
                dve.wait_ge(g_hi_done, s + 1)
                if s >= 2:
                    dve.wait_ge(down_done, s - 1)
                dve.tensor_tensor(g_lo[:, h, :], g[:, h, :], g_hi[:, h, :].bitcast(F32), ALU.subtract).then_inc(g_lo_done, 1)
                if s == 1:
                    spans()
                elif s == 2:
                    experts_of_items()
                elif s == 3:
                    tiles_of_items()
                for e in range(first + AMID[s], first + AMID[s] + BEHIND[s]):
                    late(e)
            for e in range(E - LAST, E - 2):
                late(e)
            for h in range(2):
                dve.wait_ge(down_done, 2 * NSH - 1 + h)
                for j in range(2):
                    t = TH * h + 2 * j
                    dve.scalar_tensor_tensor(out=acc[:, t:t + 2, :], in0=down_ps[h][j][:, :].rearrange("p (i d) -> p i d", i=2),
                                             scalar=1.0 / (TOP_K + 1), in1=acc[:, t:t + 2, :], op0=ALU.mult, op1=ALU.add).then_inc(added, 1)
                late(E - 2 + h)

            def pair_round(pair):
                if t := pair(2):
                    n, b, m = number(t), t[1] % 2, halves(number(t))
                    dve.wait_ge(t_g_hi, n + 1)
                    dve.tensor_tensor(tg[1][:, b, 0:m, :], gt_ps[b][:, 0:m, :], tg[0][:, b, 0:m, :].bitcast(F32),
                                      ALU.subtract).then_inc(t_g_lo, 1)
                if t := pair(0):
                    n, r, b, m = number(t), t[1], t[1] % 2, halves(number(t))
                    dve.wait_ge(t_x_hi, n + 1)
                    dve.tensor_tensor(tx[1][:, b, 0:m, :], xt_ps[b][:, 0:m, :], tx[0][:, b, 0:m, :].bitcast(F32),
                                      ALU.subtract).then_inc(t_x_lo, 1)
                    dve.tensor_copy(row_w[:, r, 0:m], xt[:, r, 0:m, D + 1]).then_inc(t_weight, 1)
                    dest = dest_i[:, bass.ds(n, 1), 0:m].rearrange("p a i -> p (a i)")
                    keys = xt[:, r, 0:m, D].bitcast(I32)
                    of_item = item_key[:, bass.ds(n, 1), 0:m].rearrange("p a i -> p (a i)")
                    dve.tensor_tensor(dest, keys, of_item, ALU.bitwise_xor).then_inc(t_dest, 1)
                if t := pair(1):
                    n, b, m = number(t), t[1] % 2, halves(number(t))
                    dve.wait_ge(t_silu, n + 1)
                    dve.tensor_tensor(t_gated[:, b, 0:m, :], t_sil[:, b, 0:m, :], gu_ps[b][:, 0:m, H:2 * H], ALU.mult).then_inc(t_g, 1)

            rounds(dve, pair_round)

            for t in range(TT):
                if t not in POOL_TILES:
                    combine(dve, t)

        @block.tensor
        def _(pe):
            pe.wait_ge(warm_ready, 1)
            for i in range(WARM):
                pe.matmul(row_ps[0][:, :], warm[:, 0:P], warm, start=True, stop=True)
            for h in range(2):
                pe.wait_ge(x_in[h], 16)
                pe.wait_ge(bd_done, Q * (h + 1))
                for k in range(KD):
                    for t in range(TH * h, TH * h + TH):
                        c = (t % TH) * P
                        last = pe.matmul(y_ps[h][k][:, c:c + P], acc[:, t, k * P:(k + 1) * P], cond_bd[:, t, :],
                                         start=True, stop=True)
                    last.then_inc(cond_done, 1)

            pe.wait_ge(wr_hi_done, 1)
            pe.wait_ge(wr_lo_done, 1)
            for h in range(2):
                n = 0
                for k in range(KD):
                    for y, ready in ((y_hi, y_hi_done), (y_lo, y_lo_done)):
                        pe.wait_ge(ready, KD * h + k + 1)
                        last = pe.matmul(lgt_ps[h], wr_pair[:, k, :, :].rearrange("p m e -> p (m e)"), y[:, k, h * HALF:(h + 1) * HALF],
                                         start=(n == 0), stop=(n == 2 * KD - 1))
                        n += 1
                last.then_inc(lgt_done, 1)

            def token_rows(j):
                for i in range(2):
                    last = pe.matmul(row_ps[j][:, i * D:(i + 1) * D], cond_bd[:, 2 * j + i, :], acc[:, 2 * j + i, :], start=True, stop=True)
                last.then_inc(row_done, 1)

            token_rows(0)
            pe.wait_ge(const_done, 10)
            pe.wait_ge(lgt_out, 2)
            for t in range(TT):
                last = pe.transpose(lg_ps[:, t * 2 * E:(t + 1) * 2 * E], lgt[:, t * P:(t + 1) * P], ident[0:2 * E, 0:2 * E])
            last.then_inc(lg_done, 1)
            for j in range(1, 4):
                token_rows(j)

            def ranks():
                pe.wait_ge(mask_done, 1)
                m = mask[:, :, :].rearrange("p t e -> p (t e)")
                pe.matmul(rank_ps[:, 0:TT * E], tri[:, :], m, start=True, stop=False, skip_group_check=True)
                for t in range(TT):
                    n = TT - t
                    last = pe.matmul(rank_ps[:, (t + 1) * E:(TT + 1) * E].rearrange("p (n e) -> p n e", e=E), ones[:, :],
                                     repeat(mask[:, t, :], n), start=False, stop=(t == TT - 1), skip_group_check=True)
                last.then_inc(rank_done, 1)

            def down(s):
                h, k = s % 2, w_slot(s // 2)
                pe.wait_ge(g_hi_done, s + 1)
                pe.wait_ge(g_lo_done, s + 1)
                if s < 2:
                    pe.wait_ge(row_out, 4)
                if s == 1:
                    pe.wait_ge(slot_done, 2)
                for j in range(2):
                    for i in range(2):
                        c = (2 * j + i) * P
                        for m, (a, b) in enumerate([(g_hi, w_hi), (g_hi, w_lo), (g_lo, w_hi)]):
                            last = pe.matmul(down_ps[h][j][:, i * D:(i + 1) * D], a[:, h, c:c + P], w2(b, k),
                                             start=(s < 2 and m == 0 and i == 0), stop=(s >= 2 * NSH - 2 and m == 2), skip_group_check=True)
                last.then_inc(down_done, 1)

            for s in range(2 * NSH):
                h, u = s % 2, s // 2
                if h == 0:
                    if u < LEAD:
                        pe.wait_ge(lead_split, u + 1)
                    else:
                        pe.wait_ge(pool_split, u - LEAD + 1)
                if s == 1:
                    ranks()
                    pe.wait_ge(row_out, 8)
                for m, (ps, free, ready) in enumerate([(gate_ps, silu_done, gate_done), (up_ps, g_done, up_done)]):
                    if s >= 2:
                        pe.wait_ge(free, s - 1)
                    n = 0
                    for kd in range(KD):
                        for a, b in [(w_hi, y_hi), (w_hi, y_lo), (w_lo, y_hi)]:
                            last = pe.matmul(ps[h][:, :], w13(a, w_slot(u), m, kd), b[:, kd, h * HALF:(h + 1) * HALF],
                                             start=(n == 0), stop=(n == 3 * KD - 1))
                            n += 1
                    last.then_inc(ready, 1)
                if s:
                    down(s - 1)
            down(2 * NSH - 1)

            def load_experts(at):
                registers = [pe.alloc_register(f"expert{len(loads)}_{i}") for i in range(4)]
                loads.append(at)
                pe.load(registers, item_e_i[0:1, bass.ds(at, 1), :].rearrange("p a n -> p (a n)"))
                return [pe.snap(r, donate=True, min_val=0, max_val=E - 1) for r in registers]

            loads = []

            def pair_round(pair):
                if t := pair(0):
                    r, b = t[1], t[1] % 2
                    pe.wait_ge(xt_in[r], t[0] * 32 + 32)
                    for i in range(halves(number(t))):
                        for k in range(KD):
                            last = pe.transpose(xt_ps[b][:, i, k * P:(k + 1) * P], xt[:, r, i, k * P:(k + 1) * P], ident[:, :])
                    last.then_inc(t_turned, 1)
                if pair(1) or pair(2):
                    experts = load_experts(number(pair(1)) if pair(1) else number(pair(2)) + 1)
                if t := pair(2):
                    n, b = number(t), t[1] % 2
                    pe.wait_ge(t_g, n + 1)
                    for i in range(halves(number(t))):
                        last = pe.transpose(gt_ps[b][:, i, :], t_gated[:, b, i, :], ident[:, :])
                    last.then_inc(t_g_turned, 1)
                if t := pair(1):
                    n, b = number(t), t[1] % 2
                    pe.wait_ge(t_x_lo, n + 1)
                    for i in range(halves(number(t))):
                        m = 0
                        for k in range(KD):
                            for a, w in [(0, w_hi), (1, w_hi), (0, w_lo)]:
                                last = pe.matmul(gu_ps[b][:, i, :], tx[a][:, b, i, k * P:(k + 1) * P],
                                                 of(w, experts[i], k * 2 * H, (k + 1) * 2 * H),
                                                 start=(m == 0), stop=(m == 3 * KD - 1))
                                m += 1
                    last.then_inc(t_gate_up, 1)
                if t := pair(2):
                    n, b = number(t), t[1] % 2
                    pe.wait_ge(t_g_lo, n + 1)
                    for i in range(halves(number(t))):
                        for m, (a, w) in enumerate([(0, w_hi), (1, w_hi), (0, w_lo)]):
                            last = pe.matmul(out_ps[b][:, i, :], tg[a][:, b, i, :], of(w, experts[2 + i], 2 * KD * H, WC),
                                             start=(m == 0), stop=(m == 2))
                    last.then_inc(t_down, 1)

            pe.wait_ge(added, 2)
            for i in range(STAY_WARM):
                pe.matmul(down_ps[0][1][:, :], warm[:, 0:P], warm, start=True, stop=True)
            pe.wait_ge(items_done, 2)
            pe.wait_ge(late_split, E - POOL_E)
            pe.wait_ge(pool_split, NSH - LEAD + POOL_E)
            pe.wait_ge(added, 4)
            rounds(pe, pair_round)

    return nc


_INS = ["x", "itok_B_1_198", "L0_cond_weights", "L0_ffn_w_router", "L0_ffn_we1", "L0_ffn_we3", "L0_ffn_we2",
        "L0_ffn_ws1", "L0_ffn_ws3", "L0_ffn_ws2"]


def kernel(**inputs):
    import concourse.bacc as bacc
    from concourse.bass_utils import run_bass_kernel_spmd

    nc = bacc.Bacc("TRN2", target_bir_lowering=False, num_devices=1)
    arrays, args = {}, []
    for name in _INS:
        a = np.ascontiguousarray(inputs[name])
        arrays[f"in_{name}"] = a
        args.append(nc.dram_tensor(f"in_{name}", a.shape, mybir.dt.from_np(a.dtype), kind="ExternalInput").ap())
    out = nc.dram_tensor("out", inputs["x"].shape, F32, kind="ExternalOutput").ap()
    adaln_ffn(nc, *args, out)
    return run_bass_kernel_spmd(nc, [arrays], core_ids=[0]).results[0]["out"]
```
